# Optimizing a Trainium2 kernel written in Bass

```python
import numpy as np
import jax
import jax.numpy as jnp

def _softmax(x, axis=-1):
    return jax.nn.softmax(x, axis=axis)

def _gelu(x):
    return jax.nn.gelu(x, approximate=True)

def _silu(x):
    return jax.nn.silu(x)

def _sigmoid(x):
    return jax.nn.sigmoid(x)

def _layernorm(x, axis=-1, eps=1e-05):
    m = jnp.mean(x, axis=axis, keepdims=True)
    v = jnp.var(x, axis=axis, keepdims=True)
    return (x - m) / jnp.sqrt(v + eps)

def _scatter_add(tgt, idx, src, axis=0):
    return tgt.at[idx].add(src)

def _segment_sum(src, seg, n):
    return jax.ops.segment_sum(src, seg, n)
kernel_name = 'mk_rec_standalone_d1_rec_r8_c248be'

def setup_inputs(seed: int=0):
    np.random.seed(seed)
    _w = jnp.asarray

    def _rec_inputs():
        import jax
        import jax.numpy as jnp
        _rk = jax.random.key(seed)
        r_feature = -0.0002422 + 0.999987 * jax.random.normal(jax.random.fold_in(_rk, 1), (512, 200, 64), jnp.float32)
        return r_feature
    r_feature = _rec_inputs()

    def _L0_rec_setup():
        import jax, jax.numpy as jnp
        import numpy as np
        B, F, E = (256, 200, 64)
        key = jax.random.key(seed)
        k1, k2 = jax.random.split(key)
        feature = jax.random.normal(k1, (B, F, E), dtype=jnp.float32)
        weight = 0.01 * jax.random.normal(k2, (F, E, E), dtype=jnp.float32)
        return {'feature': feature, 'weight': weight}
    _L0_rec_all = _L0_rec_setup()
    _L0_rec_in = {k: v for k, v in _L0_rec_all.items() if k in ('weight',)}
    del _L0_rec_all
    return {'r_feature': r_feature, 'L0_rec_weight': _L0_rec_in['weight']}

def reference(r_feature, L0_rec_weight):
    import jax
    import jax.numpy as jnp

    def _L0_rec_ref(feature, weight):
        import jax, jax.numpy as jnp
        import numpy as np
        B, F, E = (256, 200, 64)
        bilinear = jnp.einsum('bie,ied->bid', feature, weight)
        out = jnp.einsum('bid,bjd->bij', bilinear, feature)
        return out
    y = _L0_rec_ref(r_feature, L0_rec_weight)
    return y

_drawn_inputs = setup_inputs


def setup_inputs(seed=0):
    import zlib

    import numpy as np

    out = dict(_drawn_inputs(seed))
    spreads = {}
    factors = {}
    for name, (base, spread) in spreads.items():
        noise = np.random.default_rng([zlib.crc32(name.encode()), seed]).standard_normal(out[name].shape)
        drawn = base * np.exp(spread * noise) if base else spread * noise
        out[name] = jnp.asarray(drawn.astype(out[name].dtype))
    for name, factor in factors.items():
        out[name] = (out[name] * factor).astype(out[name].dtype)
    return out
```

```python
import concourse.bass as bass
from concourse import mybir

F32 = mybir.dt.float32

BATCH, FIELDS, EMB = 512, 200, 64
GROUPS = 4
HALF = BATCH // GROUPS // 2
PAIRS = HALF // 2
CHUNKS = (128, FIELDS - 128)
BANKS, BANK = 8, 512

MIX_ROWS = BANK // HALF
MIX_UNITS = tuple(c // MIX_ROWS for c in CHUNKS)
SCORE_UNITS = PAIRS
UNIT = 4 * FIELDS
TILES = SCORE_UNITS // 2
SLOTS = 4
ROUNDS = TILES // SLOTS
TAIL = CHUNKS[1] - 64

MIXES = sum(MIX_UNITS)
SCORES = 2 * SCORE_UNITS
ACT_MIXES = [sum(u // 2 % 2 == 0 for u in range(n)) for n in MIX_UNITS]
DVE_MIXES = [n - a for n, a in zip(MIX_UNITS, ACT_MIXES)]
SLOT_WRITES = ROUNDS * 16 + ROUNDS * 32

FREE = 1

W_PIECES = ((0, 16), (16, 48), (48, 88), (88, 128), (128, 200))
X_PIECES = 2


def build(nc, x, weight, out_top, out_mid, out_tail):
    sb = lambda name, shape: nc.alloc_sbuf_tensor(name, shape, F32)
    w_sb = sb("w_sb", [128, FIELDS, EMB])
    x_sb = [sb(f"x_sb{k}", [128, PAIRS, FIELDS, 2]) for k in range(2)]
    mixed = sb("mixed", [128, PAIRS, CHUNKS[0], 2])
    tile = sb("tile", [128, SLOTS, 2, 2, 2 * FIELDS])
    psum = nc.alloc_psum_tensor("psum", [128, BANKS, BANK], F32)

    sem = nc.alloc_semaphore
    w_loaded = [sem(f"w_loaded{k}") for k in range(len(W_PIECES))]
    x_loaded = [sem(f"x_loaded{k}") for k in range(2)]
    bank_free = sem("bank_free")
    mix_ready = sem("mix_ready")
    score_ready = sem("score_ready")
    mix_act = sem("mix_act")
    mix_dve = sem("mix_dve")
    score_act = sem("score_act")
    score_dve = sem("score_dve")
    slot_out = [sem(f"slot_out{k}") for k in range(SLOTS)]

    def mix_bank(u):
        return psum[:, u % BANKS, :].rearrange("p (i b s) -> p b i s", i=MIX_ROWS, s=2)

    def mixed_rows(u):
        return mixed[:, :, u * MIX_ROWS:(u + 1) * MIX_ROWS, :]

    def slot_target(g, c, k):
        return g * SLOT_WRITES + (0, ROUNDS * 16)[c] + (16, 32)[c] * k

    with nc.Block() as block:

        @block.sync
        def _(sp):
            def load_x(buffer, g):
                step = PAIRS // X_PIECES
                for n in range(X_PIECES):
                    sp.dma_start(x_sb[buffer][:, n * step:(n + 1) * step, :, :],
                                 x[g, :, n * step:(n + 1) * step, :, :]).then_inc(x_loaded[buffer], 16)

            load_x(0, 0)
            for n, (a, b) in enumerate(W_PIECES):
                for half in range(2):
                    sp.dma_start(w_sb[half * EMB:(half + 1) * EMB, a:b, :],
                                 weight[:, a:b, :]).then_inc(w_loaded[n], 16)
            load_x(1, 1)

            def write_chunk(g, c):
                with sp.Fori(0, ROUNDS) as k:
                    for s in range(SLOTS):
                        done = FREE + (g * 2 + c) * TILES + k * SLOTS + s + 1
                        sp.wait_ge(score_act, done)
                        sp.wait_ge(score_dve, done)
                        t = k * SLOTS + s
                        if c == 0:
                            sp.dma_start(out_top[g, t], tile[:, s]).then_inc(slot_out[s], 16)
                        else:
                            sp.dma_start(out_mid[g, t], tile[0:64, s]).then_inc(slot_out[s], 16)
                            sp.dma_start(out_tail[g, t], tile[64:64 + TAIL, s]).then_inc(slot_out[s], 16)

            for g in range(GROUPS):
                if 1 <= g < GROUPS - 1:
                    sp.wait_ge(score_ready, g * SCORES)
                    load_x((g + 1) % 2, g + 1)
                for c in range(2):
                    write_chunk(g, c)
            for s in range(SLOTS):
                sp.wait_ge(slot_out[s], GROUPS * SLOT_WRITES)

        @block.tensor
        def _(pe):
            def mix(g, buffer, c):
                for u in range(MIX_UNITS[c]):
                    row = CHUNKS[0] * c + u * MIX_ROWS
                    mine = u // 2 % 2 == 0
                    if u < BANKS and u % 2 == 0:
                        scored = FREE + (g * 2 + c) * TILES
                        pe.wait_ge(score_act if mine else score_dve, scored)
                        pe.sem_inc(bank_free, 1)
                    elif u >= BANKS:
                        before = u - BANKS
                        own = before // 4 * 2 + before % 2 + 1
                        total = ACT_MIXES if mine else DVE_MIXES
                        pe.wait_ge(mix_act if mine else mix_dve, g * sum(total) + c * total[0] + own)
                        pe.sem_inc(bank_free, 1)
                    for n, (a, b) in enumerate(W_PIECES):
                        if a <= row < b:
                            pe.wait_ge(w_loaded[n], 32)
                    for r in range(MIX_ROWS):
                        i = row + r
                        for h in range(2):
                            rows = slice(h * EMB, (h + 1) * EMB)
                            last = nc.tensor.matmul(psum[rows, u % BANKS, r * HALF:(r + 1) * HALF],
                                                    w_sb[rows, i, :], x_sb[buffer][rows, :, i, :],
                                                    start=True, stop=True)
                    last.then_inc(mix_ready, 1)

            def score(g, buffer, c):
                pe.wait_ge(mix_act, g * sum(ACT_MIXES) + sum(ACT_MIXES[:c + 1]))
                pe.wait_ge(mix_dve, g * sum(DVE_MIXES) + sum(DVE_MIXES[:c + 1]))
                for q in range(SCORE_UNITS):
                    if q >= 4:
                        done = FREE + (g * 2 + c) * TILES + (q - 4) // 2 + 1
                        pe.wait_ge(score_act if q % 2 == 0 else score_dve, done)
                    for s in range(2):
                        for h in range(2):
                            rows = slice(h * EMB, (h + 1) * EMB)
                            last = nc.tensor.matmul(
                                psum[0:CHUNKS[c], q % 4 * 2 + h, s * FIELDS:(s + 1) * FIELDS],
                                mixed[rows, q, 0:CHUNKS[c], s], x_sb[buffer][rows, q, :, s],
                                start=True, stop=True)
                    last.then_inc(score_ready, 1)

            with pe.Fori(0, GROUPS // 2) as pair:
                for buffer in range(2):
                    g = pair * 2 + buffer
                    pe.wait_ge(x_loaded[buffer], (pair + 1) * (16 * X_PIECES))
                    for c in range(2):
                        mix(g, buffer, c)
                        score(g, buffer, c)

        def copies(eng, copy, first, mix_done, score_done):
            def copy_mix(g, c):
                for u in range(MIX_UNITS[c]):
                    if u // 2 % 2 == first:
                        eng.wait_ge(mix_ready, g * MIXES + c * MIX_UNITS[0] + u + 1)
                        copy(mixed_rows(u), mix_bank(u)).then_inc(mix_done, 1)

            def copy_scores(g, c, k, slots_used=True):
                for s in range(SLOTS):
                    q = 2 * s + first
                    unit = (g * 2 + c) * SCORE_UNITS + k * (2 * SLOTS) + q + 1
                    eng.wait_ge(score_ready, unit)
                    if slots_used:
                        eng.wait_ge(slot_out[s], slot_target(g, c, k))
                    copy(tile[0:CHUNKS[c], s, first],
                         psum[0:CHUNKS[c], q % 4 * 2:q % 4 * 2 + 2, 0:2 * FIELDS]).then_inc(score_done, 1)

            def copy_chunk(g, c):
                copy_mix(g, c)
                with eng.Fori(0, ROUNDS) as k:
                    copy_scores(g, c, k)

            eng.sem_inc(score_done, FREE)
            copy_mix(0, 0)
            copy_scores(0, 0, 0, slots_used=False)
            with eng.Fori(1, ROUNDS) as k:
                copy_scores(0, 0, k)
            copy_chunk(0, 1)
            with eng.Fori(1, GROUPS) as g:
                for c in range(2):
                    copy_chunk(g, c)

        @block.scalar
        def _(act):
            copies(act, nc.scalar.copy, 0, mix_act, score_act)

        @block.vector
        def _(dve):
            copies(dve, nc.vector.tensor_copy, 1, mix_dve, score_dve)


def kernel(r_feature, L0_rec_weight):
    import numpy as np
    import concourse.bacc as bacc
    from concourse.bass_utils import run_bass_kernel_spmd

    x = np.ascontiguousarray(
        np.asarray(r_feature).reshape(GROUPS, 2, PAIRS, 2, FIELDS, EMB).transpose(0, 1, 5, 2, 4, 3)
    ).reshape(GROUPS, 128, PAIRS, FIELDS, 2)
    w = np.ascontiguousarray(np.asarray(L0_rec_weight).transpose(1, 0, 2))

    nc = bacc.Bacc("TRN2", target_bir_lowering=False, num_devices=1)
    rows = (CHUNKS[0], 64, TAIL)
    shapes = [(GROUPS, TILES, r, 2, 2, 2 * FIELDS) for r in rows]
    args = [nc.dram_tensor("x_dram", x.shape, F32, kind="ExternalInput").ap(),
            nc.dram_tensor("w_dram", w.shape, F32, kind="ExternalInput").ap()]
    args += [nc.dram_tensor(f"out{n}_dram", s, F32, kind="ExternalOutput").ap() for n, s in enumerate(shapes)]
    build(nc, *args)
    r = run_bass_kernel_spmd(nc, [{"x_dram": x, "w_dram": w}], core_ids=[0]).results[0]

    out = np.concatenate([r[f"out{n}_dram"] for n in range(3)], axis=2)
    out = out.reshape(GROUPS, TILES, FIELDS, 2, 2, 2, FIELDS).transpose(0, 4, 1, 3, 5, 2, 6)
    return np.ascontiguousarray(out).reshape(BATCH, FIELDS, FIELDS)
```

```python
import concourse.bass as bass
from concourse import mybir

F32 = mybir.dt.float32

BATCH, FIELDS, EMB = 512, 200, 64
GROUPS = 4
QUADS = BATCH // GROUPS // 4
SAMPLES = 4 * QUADS
TOP, MID, TAIL = 128, 64, 8
TAIL_TILE = 32
LOW_ROWS, TOP_ROWS = range(TOP, FIELDS), range(0, TOP)

BANK = 512
BANK_PAIRS = 4
TWO = 2 * FIELDS

MIX_UNIT = 2 * 2 * BANK // SAMPLES
MIX_UNITS = {"low": -(-len(LOW_ROWS) // MIX_UNIT), "top": len(TOP_ROWS) // MIX_UNIT}
MIX_COPIES = 4

UNITS = {"mid": QUADS // 2, "tail": QUADS // 4, "top": QUADS}
SLOTS = 4
ROUNDS = {part: units // 2 // SLOTS for part, units in UNITS.items()}
DMAS = {"mid": 1, "tail": 4, "top": 1}
PARTS = ("mid", "tail", "top")

MIXES = sum(MIX_UNITS.values())
SCORES = sum(UNITS.values())
ENGINE_SCORES = SCORES // 2
SLOT_OUTS = 16 * sum(ROUNDS[p] * DMAS[p] for p in PARTS)
FREE = 1

W_PIECES = ((128, 200), (0, 128))
X_QUADS = 4
X_LOADS = 16 * 2 * QUADS // X_QUADS


def scores_before(part):
    return sum(UNITS[p] for p in PARTS[:PARTS.index(part)])


def outs_before(part):
    return 16 * sum(ROUNDS[p] * DMAS[p] for p in PARTS[:PARTS.index(part)])


def mix_units(chunk):
    rows = LOW_ROWS if chunk == "low" else TOP_ROWS
    for u in range(MIX_UNITS[chunk]):
        first = rows[0] + u * MIX_UNIT
        yield u, first, min(MIX_UNIT, rows[-1] + 1 - first) // 2


def engine_mixes(chunk, engine, before=None):
    return MIX_COPIES * sum(u % 2 == engine for u in range(MIX_UNITS[chunk] if before is None else before))


def build(nc, x, weight, out_top, out_mid, out_tail):
    sb = lambda name, shape: nc.alloc_sbuf_tensor(name, shape, F32)
    w_sb = sb("w_sb", [128, FIELDS, EMB])
    x_sb = sb("x_sb", [128, QUADS, 2, FIELDS, 2])
    mixed = sb("mixed", [128, QUADS, TOP, 2])
    tile = sb("tile", [128, SLOTS, 2, 2, TWO])
    psum = nc.alloc_psum_tensor("psum", [128, 2 * BANK_PAIRS, BANK], F32)

    sem = nc.alloc_semaphore
    zeroed = sem("zeroed")
    w_loaded = [sem(f"w_loaded{n}") for n in range(len(W_PIECES))]
    x_loaded = sem("x_loaded")
    mix_ready = sem("mix_ready")
    score_ready = sem("score_ready")
    mix_copied = [sem("mix_act"), sem("mix_dve")]
    score_copied = [sem("score_act"), sem("score_dve")]
    slot_out = [sem(f"slot_out{s}") for s in range(SLOTS)]

    with nc.Block() as block:

        @block.sync
        def _(sp):
            def load_x(g, quad):
                for half in range(2):
                    sp.dma_start(x_sb[half * EMB:(half + 1) * EMB, quad:quad + X_QUADS, half, :, :],
                                 x[g, half, :, quad:quad + X_QUADS, :, :]).then_inc(x_loaded, 16)

            def write_tile(g, part, t, s, reload=None):
                done = FREE + g * ENGINE_SCORES + scores_before(part) // 2 + t + 1
                sp.wait_ge(score_copied[0], done)
                sp.wait_ge(score_copied[1], done)
                if reload is not None:
                    load_x(g + 1, reload)
                if part == "tail":
                    for c in range(4):
                        last = TAIL_TILE * (c + 1)
                        sp.dma_start(out_tail[g, t, c], tile[last - TAIL:last, s]).then_inc(slot_out[s], 16)
                else:
                    out = out_top if part == "top" else out_mid
                    sp.dma_start(out[g, t], tile[:, s]).then_inc(slot_out[s], 16)

            def write_low(g):
                with sp.Fori(0, ROUNDS["mid"]) as k:
                    for s in range(SLOTS):
                        write_tile(g, "mid", k * SLOTS + s, s)
                for s in range(SLOTS):
                    write_tile(g, "tail", s, s)

            for quad in range(0, QUADS, X_QUADS):
                load_x(0, quad)
            for n, (a, b) in enumerate(W_PIECES):
                for half in range(2):
                    sp.dma_start(w_sb[half * EMB:(half + 1) * EMB, a:b, :],
                                 weight[:, a:b, :]).then_inc(w_loaded[n], 16)
            with sp.Fori(0, GROUPS - 1) as g:
                write_low(g)
                for k in range(ROUNDS["top"]):
                    for s in range(SLOTS):
                        t = k * SLOTS + s
                        last_use = (2 * t + 2) % X_QUADS == 0
                        write_tile(g, "top", t, s, reload=2 * t + 2 - X_QUADS if last_use else None)
            write_low(GROUPS - 1)
            with sp.Fori(0, ROUNDS["top"]) as k:
                for s in range(SLOTS):
                    write_tile(GROUPS - 1, "top", k * SLOTS + s, s)
            for s in range(SLOTS):
                sp.wait_ge(slot_out[s], GROUPS * SLOT_OUTS)

        @block.tensor
        def _(pe):
            def mix(g, chunk):
                pe.wait_ge(w_loaded[0 if chunk == "low" else 1], 32)
                for u, first, rows in mix_units(chunk):
                    engine = u % 2
                    if u < BANK_PAIRS:
                        before = g * ENGINE_SCORES + (0 if chunk == "low" else scores_before("top") // 2)
                        pe.wait_ge(score_copied[engine], FREE + before)
                    else:
                        before = g * (engine_mixes("low", engine) + engine_mixes("top", engine))
                        before += engine_mixes("low", engine) if chunk == "top" else 0
                        pe.wait_ge(mix_copied[engine], before + engine_mixes(chunk, engine, u - BANK_PAIRS + 1))
                    for r in range(rows):
                        for c in range(2):
                            bank = u % BANK_PAIRS * 2 + r // 4
                            last = nc.tensor.matmul(
                                psum[c * EMB:(c + 1) * EMB, bank, r % 4 * SAMPLES:(r % 4 + 1) * SAMPLES],
                                w_sb[:, first + c * rows + r, :], x_sb[:, :, :, first + c * rows + r, :],
                                start=True, stop=True)
                    last.then_inc(mix_ready, 1)

            def score(g, part, matmuls):
                chunk = "top" if part == "top" else "low"
                for engine in range(2):
                    done = g * (engine_mixes("low", engine) + engine_mixes("top", engine))
                    done += engine_mixes("low", engine) + (engine_mixes("top", engine) if chunk == "top" else 0)
                    pe.wait_ge(mix_copied[engine], done)
                for u in range(UNITS[part]):
                    if part == "tail" or u >= BANK_PAIRS:
                        done = g * ENGINE_SCORES + (scores_before(part) + u - BANK_PAIRS) // 2 + 1
                        pe.wait_ge(score_copied[u % 2], FREE + done)
                    for bank, partition, rows, quad, pair in matmuls(u):
                        last = nc.tensor.matmul(
                            psum[partition:partition + len(rows), u % BANK_PAIRS * 2 + bank, 0:TWO],
                            mixed[:, quad, rows[0]:rows[-1] + 1, pair], x_sb[:, quad, :, :, pair],
                            start=True, stop=True)
                    last.then_inc(score_ready, 1)

            def mid_matmuls(u):
                return [(a, pair * MID, range(MID), 2 * u + a, pair) for a in range(2) for pair in range(2)]

            def tail_matmuls(u):
                rows = range(MID + TAIL - TAIL_TILE, MID + TAIL)
                return [(a, (2 * q + pair) * TAIL_TILE, rows, 4 * u + 2 * a + q, pair)
                        for a in range(2) for q in range(2) for pair in range(2)]

            def top_matmuls(u):
                return [(pair, 0, range(TOP), u, pair) for pair in range(2)]

            pe.wait_ge(zeroed, 2)
            with pe.Fori(0, GROUPS) as g:
                pe.wait_ge(x_loaded, (g + 1) * X_LOADS)
                mix(g, "low")
                score(g, "mid", mid_matmuls)
                score(g, "tail", tail_matmuls)
                mix(g, "top")
                score(g, "top", top_matmuls)

        def copies(eng, copy, engine):
            def copy_mix(g, chunk):
                for u, first, rows in mix_units(chunk):
                    if u % 2 != engine:
                        continue
                    ready = g * MIXES + (MIX_UNITS["low"] if chunk == "top" else 0) + u + 1
                    eng.wait_ge(mix_ready, ready)
                    bank = u % BANK_PAIRS * 2
                    for c in range(2):
                        source = psum[c * EMB:(c + 1) * EMB, bank:bank + 2, :].rearrange(
                            "p b (r q h s) -> p q h (b r) s", r=BANK // SAMPLES, q=QUADS, h=2)
                        i = first + c * rows - (TOP if chunk == "low" else 0)
                        for half in range(2):
                            copy(mixed[half * EMB:(half + 1) * EMB, :, i:i + rows, :],
                                 source[:, :, half, 0:rows, :]).then_inc(mix_copied[engine], 1)

            def copy_scores(g, part, k, slots_used=True):
                for s in range(SLOTS):
                    u = 2 * s + engine
                    ready = g * SCORES + scores_before(part) + k * (2 * SLOTS) + u + 1
                    eng.wait_ge(score_ready, ready)
                    if slots_used:
                        out = g * SLOT_OUTS + outs_before(part) + k * (16 * DMAS[part])
                        eng.wait_ge(slot_out[s], out)
                    bank = u % BANK_PAIRS * 2
                    copy(tile[:, s, engine], psum[:, bank:bank + 2, 0:TWO]).then_inc(score_copied[engine], 1)

            def copy_rounds(g, part, first=0):
                with eng.Fori(first, ROUNDS[part]) as k:
                    copy_scores(g, part, k)

            def copy_rest(g):
                copy_scores(g, "tail", 0)
                copy_mix(g, "top")
                copy_rounds(g, "top")

            eng.sem_inc(score_copied[engine], FREE)
            copy_mix(0, "low")
            copy_scores(0, "mid", 0, slots_used=False)
            copy_rounds(0, "mid", first=1)
            copy_rest(0)
            with eng.Fori(1, GROUPS) as g:
                copy_mix(g, "low")
                copy_rounds(g, "mid")
                copy_rest(g)

        @block.scalar
        def _(act):
            copies(act, nc.scalar.copy, 0)

        @block.vector
        def _(dve):
            nc.vector.memset(x_sb[0:EMB, :, 1, :, :], 0.0).then_inc(zeroed, 1)
            copies(dve, nc.vector.tensor_copy, 1)

        @block.gpsimd
        def _(pool):
            nc.gpsimd.memset(x_sb[EMB:128, :, 0, :, :], 0.0).then_inc(zeroed, 1)


def kernel(r_feature, L0_rec_weight):
    import numpy as np
    import concourse.bacc as bacc
    from concourse.bass_utils import run_bass_kernel_spmd

    x = np.asarray(r_feature).reshape(GROUPS, 2, QUADS, 2, FIELDS, EMB)
    x = np.ascontiguousarray(x.transpose(0, 1, 5, 2, 4, 3))
    w = np.ascontiguousarray(np.asarray(L0_rec_weight).transpose(1, 0, 2))

    nc = bacc.Bacc("TRN2", target_bir_lowering=False, num_devices=1)
    shapes = {
        "top": (GROUPS, QUADS // 2, TOP, 2, 2, TWO),
        "mid": (GROUPS, QUADS // 4, 2 * MID, 2, 2, TWO),
        "tail": (GROUPS, QUADS // 8, 4, TAIL, 2, 2, TWO),
    }
    args = [nc.dram_tensor("x_dram", x.shape, F32, kind="ExternalInput").ap(),
            nc.dram_tensor("w_dram", w.shape, F32, kind="ExternalInput").ap()]
    args += [nc.dram_tensor(f"out_{n}_dram", s, F32, kind="ExternalOutput").ap() for n, s in
             ((n, shapes[n]) for n in ("top", "mid", "tail"))]
    build(nc, *args)
    r = run_bass_kernel_spmd(nc, [{"x_dram": x, "w_dram": w}], core_ids=[0]).results[0]

    top = r["out_top_dram"].reshape(GROUPS, QUADS // 2, TOP, 2, 2, 2, FIELDS)
    top = top.transpose(0, 5, 1, 3, 4, 2, 6).reshape(GROUPS, 2, QUADS, 2, TOP, FIELDS)
    mid = r["out_mid_dram"].reshape(GROUPS, QUADS // 4, 2, MID, 2, 2, 2, FIELDS)
    mid = mid.transpose(0, 6, 1, 4, 5, 2, 3, 7).reshape(GROUPS, 2, QUADS, 2, MID, FIELDS)
    tail = r["out_tail_dram"].reshape(GROUPS, QUADS // 8, 2, 2, TAIL, 2, 2, 2, FIELDS)
    tail = tail.transpose(0, 7, 1, 5, 6, 2, 3, 4, 8).reshape(GROUPS, 2, QUADS, 2, TAIL, FIELDS)
    return np.concatenate([top, mid, tail], axis=4).reshape(BATCH, FIELDS, FIELDS)
```
